# Optimizing a Trainium2 kernel written in Bass

```python
import numpy as np
import jax
import jax.numpy as jnp

def _softmax(x, axis=-1):
    return jax.nn.softmax(x, axis=axis)

def _gelu(x):
    return jax.nn.gelu(x, approximate=True)

def _silu(x):
    return jax.nn.silu(x)

def _sigmoid(x):
    return jax.nn.sigmoid(x)

def _layernorm(x, axis=-1, eps=1e-05):
    m = jnp.mean(x, axis=axis, keepdims=True)
    v = jnp.var(x, axis=axis, keepdims=True)
    return (x - m) / jnp.sqrt(v + eps)

def _scatter_add(tgt, idx, src, axis=0):
    return tgt.at[idx].add(src)

def _segment_sum(src, seg, n):
    return jax.ops.segment_sum(src, seg, n)
kernel_name = 'mk_adaln_ffn_d1_seqx_r4_145234'

def setup_inputs(seed: int=0):
    np.random.seed(seed)
    _w = jnp.asarray

    def _rec_inputs():
        import jax
        import jax.numpy as jnp
        _rk = jax.random.key(seed)
        x = -7.109e-05 + 0.9999 * jax.random.normal(jax.random.fold_in(_rk, 1), (128, 64, 1024), jnp.float32)
        _lenS = 64 - jax.random.randint(jax.random.fold_in(_rk, 7), (128,), 0, max(1, 64 // 4) + 1, jnp.int32)
        _lenS2 = 64 - jax.random.randint(jax.random.fold_in(_rk, 8), (128,), 0, max(1, 64 // 4) + 1, jnp.int32)
        itok_B_0_15 = jax.random.randint(jax.random.fold_in(_rk, 11), (128,), 0, 16, jnp.int32)
        return (x, itok_B_0_15)
    x, itok_B_0_15 = _rec_inputs()

    def _L0_cond_setup():
        import jax, jax.numpy as jnp
        import numpy as np
        NUM_CONDITIONS = 16
        IN_CH = 64
        OUT_CH = 64
        B = 64
        T = 1024
        key = jax.random.key(seed)
        k_x, k_w, k_c = jax.random.split(key, 3)
        x = jax.random.normal(k_x, (B, IN_CH, T), dtype=jnp.float32)
        bound = float(np.sqrt(6.0 / IN_CH))
        weights = jax.random.uniform(k_w, (NUM_CONDITIONS, IN_CH, OUT_CH), dtype=jnp.float32, minval=-bound, maxval=bound)
        condition = jax.random.randint(k_c, (B,), 0, NUM_CONDITIONS, dtype=jnp.int64)
        return {'x': x, 'weights': weights, 'condition': condition}
    _L0_cond_all = _L0_cond_setup()
    _L0_cond_in = {k: v for k, v in _L0_cond_all.items() if k in ('weights',)}
    del _L0_cond_all

    def _L0_ffn_setup():
        import jax, jax.numpy as jnp
        import numpy as np
        C_CLAMP = 0.5
        EPS = 1e-06
        key = jax.random.key(seed)
        ks = jax.random.split(key, 6)
        B_, S, D, O, R, E = (4, 512, 1024, 1024, 16, 8)
        x = jax.random.normal(ks[0], (B_, S, D), dtype=jnp.float32)
        W = jax.random.normal(ks[1], (O, D), dtype=jnp.float32) * (1.0 / np.sqrt(D))
        b = jax.random.normal(ks[2], (O,), dtype=jnp.float32) * 0.01
        A = jax.random.normal(ks[3], (E, D, R), dtype=jnp.float32) * (1.0 / np.sqrt(D))
        Bm = jax.random.normal(ks[4], (E, R, O), dtype=jnp.float32) * (1.0 / np.sqrt(R))
        p_scores = jax.random.uniform(ks[5], (E,), dtype=jnp.float32)
        return {'x': x, 'W': W, 'b': b, 'A': A, 'B': Bm, 'p_scores': p_scores}
    _L0_ffn_all = _L0_ffn_setup()
    _L0_ffn_in = {k: v for k, v in _L0_ffn_all.items() if k in ('W', 'b', 'A', 'B', 'p_scores')}
    del _L0_ffn_all
    return {'x': x, 'itok_B_0_15': itok_B_0_15, 'L0_cond_weights': _L0_cond_in['weights'], 'L0_ffn_W': _L0_ffn_in['W'], 'L0_ffn_b': _L0_ffn_in['b'], 'L0_ffn_A': _L0_ffn_in['A'], 'L0_ffn_B': _L0_ffn_in['B'], 'L0_ffn_p_scores': _L0_ffn_in['p_scores']}

def reference(x, itok_B_0_15, L0_cond_weights, L0_ffn_W, L0_ffn_b, L0_ffn_A, L0_ffn_B, L0_ffn_p_scores):
    import jax
    import jax.numpy as jnp

    def _L0_cond_ref(x, weights, condition):
        import jax, jax.numpy as jnp
        import numpy as np
        NUM_CONDITIONS = 16
        IN_CH = 64
        OUT_CH = 64
        B = 64
        T = 1024
        W = weights[condition]
        return jnp.einsum('bct,bcd->bdt', x, W)

    def _L0_ffn_ref(x, W, b, A, B, p_scores):
        import jax, jax.numpy as jnp
        import numpy as np
        C_CLAMP = 0.5
        EPS = 1e-06
        z = jnp.einsum('bsd,od->bso', x, W) + b
        u = jnp.einsum('bsd,edr->ebsr', x, A)
        m = jnp.einsum('ebsr,ero,e->bso', u, B, p_scores)
        norm_z = jnp.linalg.norm(z, axis=-1, keepdims=True)
        norm_m = jnp.linalg.norm(m, axis=-1, keepdims=True)
        gamma = jnp.minimum(C_CLAMP * norm_z / (norm_m + EPS), 1.0)
        return z + gamma * m
    x = x + _L0_ffn_ref(_L0_cond_ref(x, L0_cond_weights, itok_B_0_15), L0_ffn_W, L0_ffn_b, L0_ffn_A, L0_ffn_B, L0_ffn_p_scores)
    return x

_drawn_inputs = setup_inputs


def setup_inputs(seed=0):
    import zlib

    import numpy as np

    out = dict(_drawn_inputs(seed))
    spreads = {}
    factors = {'L0_ffn_b': 8.0}
    for name, (base, spread) in spreads.items():
        noise = np.random.default_rng([zlib.crc32(name.encode()), seed]).standard_normal(out[name].shape)
        drawn = base * np.exp(spread * noise) if base else spread * noise
        out[name] = jnp.asarray(drawn.astype(out[name].dtype))
    for name, factor in factors.items():
        out[name] = (out[name] * factor).astype(out[name].dtype)
    return out
```

```python
import concourse.bass as bass
from concourse import mybir
from contextlib import ExitStack


def conditioned_clamped_low_rank_linear_kernel(
    nc: bass.Bass,
    x: bass.AP,
    condition: bass.AP,
    cond_w: bass.AP,
    w: bass.AP,
    b: bass.AP,
    a: bass.AP,
    bm: bass.AP,
    p_scores: bass.AP,
    out: bass.AP,
):
    fp32 = mybir.dt.float32
    fp32r = mybir.dt.float32r
    bf16 = mybir.dt.bfloat16
    i32 = mybir.dt.int32
    ALU = mybir.AluOpType
    ACT = mybir.ActivationFunctionType

    B, C, D = x.shape
    E = cond_w.shape[0]
    X, _, R = a.shape
    P = 128
    PER = P // C
    TILES = B // PER
    KC = D // P
    HC = KC // 2
    H = D // 2
    XR = X * R
    BODY = 4
    STEPS = TILES // BODY
    CLAMP, EPS = 0.5, 1e-6
    assert (C * PER, XR, H, D % P, TILES % BODY) == (P, P, 512, 0, 0) and STEPS >= 3

    x_tiles = x.rearrange("(n q) c t -> n (q c) t", q=PER)
    out_tiles = out.rearrange("(n q) c t -> n (q c) t", q=PER)

    ctx = ExitStack()
    with ctx:
        def sb(name, shape, dt):
            return ctx.enter_context(nc.sbuf_tensor(name, shape, dt))

        def pb(name, shape):
            return ctx.enter_context(nc.psum_tensor(name, shape, fp32))

        def sem(name):
            return ctx.enter_context(nc.semaphore(name))

        w_hi = sb("w_hi", [P, KC, D], fp32r)
        w_lo = sb("w_lo", [P, KC, D], fp32r)
        a_hi = sb("a_hi", [P, KC, XR], fp32r)
        a_lo = sb("a_lo", [P, KC, XR], fp32r)
        b_hi = sb("b_hi", [P, D], fp32r)
        b_lo = sb("b_lo", [P, D], fp32r)
        cond_all = sb("cond_all", [P, E, 2, C], fp32r)
        mixer = sb("mixer", [P, 2, 2, P], fp32r)
        bias = sb("bias", [P, D], fp32)
        cond_ids = sb("cond_ids", [1, B], i32)
        p_col = sb("p_col", [P, 1], fp32)
        ident = sb("ident", [P, P], fp32)

        x_in = sb("x_in", [P, BODY, D], fp32)
        x_hi = sb("x_hi", [P, 2, D], fp32r)
        x_lo = sb("x_lo", [P, 2, D], fp32r)
        y_hi = sb("y_hi", [P, 2, KC, 2 * P], fp32r)
        y_lo = sb("y_lo", [P, 2, KC, 2 * P], fp32r)
        u_hi = sb("u_hi", [P, 2 * P], fp32r)
        u_lo = sb("u_lo", [P, 2 * P], fp32r)
        rows = sb("rows", [P, 4, D], fp32)
        w_late = sb("w_late", [P, 4, D], fp32)
        bm_in = sb("bm_in", [P, D], fp32)
        squares = sb("squares", [P, D], bf16)
        z_sq = sb("z_sq", [P, 2, 2], fp32)
        z_sum = sb("z_sum", [P, 2], fp32)
        half = sb("half", [P, 1], fp32)
        m_sq = sb("m_sq", [P, 2], fp32)
        norm_z = sb("norm_z", [P, 2], fp32)
        norm_m = sb("norm_m", [P, 2], fp32)
        twice_m = sb("twice_m", [P, 2], fp32)
        half_over_m = sb("half_over_m", [P, 2], fp32)
        gamma = sb("gamma", [P, 2], fp32)

        z_b = rows[:, 0:2, :]
        result = rows[:, 2:4, :]
        w_early = rows[:, :, :]
        cond_in = x_in[:, 2, 0:E * C]
        a_in = x_in[:, 3, 0:KC * XR].rearrange("p (k n) -> p k n", k=KC)

        mix_ps = [pb(f"mix_ps{h}", [P, H]) for h in range(2)]
        z_ps = [pb(f"z_ps{h}", [P, H]) for h in range(2)]
        m_ps = pb("m_ps", [P, 2 * H])
        u_ps = pb("u_ps", [P, H])
        turn_ps = [z_ps[1][:, :], m_ps[:, 0:H], m_ps[:, H:2 * H]]

        x_loaded = [sem(f"x_loaded{s}") for s in range(BODY)]
        out_stored = [sem(f"out_stored{s}") for s in range(2)]
        w_loaded = [sem(f"w_loaded{n}") for n in range(8)]
        ids_loaded = sem("ids_loaded")
        cond_loaded = sem("cond_loaded")
        a_loaded = sem("a_loaded")
        bm_loaded = sem("bm_loaded")
        p_loaded = sem("p_loaded")
        bias_loaded = sem("bias_loaded")
        ones_set = sem("ones_set")
        ident_set = sem("ident_set")
        half_set = sem("half_set")
        mixer_zeroed = sem("mixer_zeroed")
        w_turned = sem("w_turned")
        w_hi_ready = sem("w_hi_ready")
        w_lo_ready = sem("w_lo_ready")
        cond_hi_ready = sem("cond_hi_ready")
        cond_lo_ready = sem("cond_lo_ready")
        a_hi_ready = sem("a_hi_ready")
        a_lo_ready = sem("a_lo_ready")
        bm_scaled = sem("bm_scaled")
        b_hi_ready = sem("b_hi_ready")
        b_lo_ready = sem("b_lo_ready")
        x_hi_ready = sem("x_hi_ready")
        x_lo_ready = sem("x_lo_ready")
        mixer_ready = sem("mixer_ready")
        mix_done = sem("mix_done")
        y_hi_ready = sem("y_hi_ready")
        y_lo_ready = sem("y_lo_ready")
        u_done = sem("u_done")
        u_hi_ready = sem("u_hi_ready")
        u_lo_ready = sem("u_lo_ready")
        z_done = sem("z_done")
        z_b_ready = sem("z_b_ready")
        z_squared = sem("z_squared")
        m_done = sem("m_done")
        m_squared = sem("m_squared")
        norm_m_ready = sem("norm_m_ready")
        norm_z_ready = sem("norm_z_ready")
        z_sum_ready = sem("z_sum_ready")
        residual_ready = sem("residual_ready")
        twice_m_ready = sem("twice_m_ready")
        over_m_ready = sem("over_m_ready")
        gamma_ready = sem("gamma_ready")
        out_ready = sem("out_ready")

        def steps(engine, step):
            step(0, True, False)
            with engine.Fori(1, STEPS - 1) as i:
                step(i, False, False)
            step(STEPS - 1, False, True)

        block = ctx.enter_context(nc.Block())

        @block.sync
        def _(sp):
            sp.dma_start(cond_ids[:, :], condition.rearrange("(o n) -> o n", o=1)).then_inc(ids_loaded, 16)
            for n in range(4):
                sp.dma_start(w_early[:, n, :], w[n * P:(n + 1) * P, :]).then_inc(w_loaded[n], 16)
            sp.dma_start(x_in[:, 0, :], x_tiles[0]).then_inc(x_loaded[0], 16)
            sp.dma_start(x_in[:, 1, :], x_tiles[1]).then_inc(x_loaded[1], 16)
            for n in range(4):
                sp.dma_start(w_late[:, n, :], w[(n + 4) * P:(n + 5) * P, :]).then_inc(w_loaded[4 + n], 16)
            sp.wait_ge(cond_lo_ready, 1)
            sp.dma_start(x_in[:, 2, :], x_tiles[2]).then_inc(x_loaded[2], 16)
            sp.wait_ge(a_lo_ready, 1)
            sp.dma_start(x_in[:, 3, :], x_tiles[3]).then_inc(x_loaded[3], 16)

            def step(i, first, last):
                for j in range(BODY):
                    t = i * BODY + j
                    if not last:
                        sp.wait_ge(residual_ready, 2 * t + 2)
                        sp.dma_start(x_in[:, j, :], x_tiles[t + BODY]).then_inc(x_loaded[j], 16)
                    sp.wait_ge(out_ready, t + 1)
                    sp.dma_start(out_tiles[t], result[:, j % 2, :]).then_inc(out_stored[j % 2], 16)

            steps(sp, step)
            for s in range(2):
                sp.wait_ge(out_stored[s], 16 * (TILES // 2))

        @block.gpsimd
        def _(pool):
            pool.dma_start(bm_in[:, :], bm.rearrange("e r o -> (e r) o")).then_inc(bm_loaded, 16)
            pool.dma_start(p_col[:, :], p_scores.rearrange("(e o) -> e o", o=1).unsqueeze(1)
                           .to_broadcast([X, R, 1])).then_inc(p_loaded, 16)
            pool.dma_start(bias[:, :], b.rearrange("(o n) -> o n", o=1).to_broadcast([P, D])).then_inc(bias_loaded, 16)
            nc.gpsimd.memset(ident[:, :], 1.0).then_inc(ones_set, 1)
            pool.wait_ge(ones_set, 1)
            nc.gpsimd.affine_select(out=ident[:, :], in_=ident[:, :], pattern=[[-1, P]], compare_op=ALU.is_equal,
                                    fill=0.0, base=0, channel_multiplier=1).then_inc(ident_set, 1)
            nc.gpsimd.memset(half[:, :], 0.5).then_inc(half_set, 1)
            nc.gpsimd.memset(mixer[:, :, :, :].bitcast(fp32), 0.0).then_inc(mixer_zeroed, 1)

            def split_lo(j):
                return nc.gpsimd.tensor_tensor(x_lo[:, j % 2, :], x_in[:, j % BODY, :],
                                               x_hi[:, j % 2, :].bitcast(fp32), ALU.subtract)

            pool.wait_ge(half_set, 1)
            for t in range(3):
                if t == 2:
                    pool.wait_ge(mix_done, 2)
                pool.wait_ge(x_hi_ready, t + 1)
                split_lo(t).then_inc(x_lo_ready, 1)

            def step(i, first, last):
                for j in range(BODY):
                    t = i * BODY + j
                    one = slice(j % 2, j % 2 + 1)

                    def residual(h):
                        cols = slice(h * H, (h + 1) * H)
                        pool.wait_ge(z_b_ready, 2 * t + h + 1)
                        nc.gpsimd.tensor_tensor(result[:, j % 2, cols], z_b[:, j % 2, cols], x_in[:, j, cols],
                                                ALU.add).then_inc(residual_ready, 1)

                    if not first or j >= 2:
                        pool.wait_ge(out_stored[j % 2], 16 * (2 * i + j // 2))
                    residual(0)
                    if not last or j + 3 < BODY:
                        pool.wait_ge(mix_done, 2 * t + 4)
                        pool.wait_ge(x_hi_ready, t + 4)
                        split_lo(j + 3).then_inc(x_lo_ready, 1)
                    pool.wait_ge(m_squared, t + 1)
                    nc.gpsimd.tensor_tensor(norm_m[:, one], m_sq[:, one], half[:, :], ALU.pow).then_inc(norm_m_ready, 1)
                    residual(1)
                    pool.wait_ge(z_squared, 2 * t + 2)
                    nc.gpsimd.tensor_tensor(z_sum[:, one], z_sq[:, j % 2, 0:1], z_sq[:, j % 2, 1:2],
                                            ALU.add).then_inc(z_sum_ready, 1)
                    pool.wait_ge(z_sum_ready, t + 1)
                    nc.gpsimd.tensor_tensor(norm_z[:, one], z_sum[:, one], half[:, :], ALU.pow).then_inc(norm_z_ready, 1)

            steps(pool, step)

        @block.scalar
        def _(act):
            for q in range(PER):
                act.dma_start(cond_in[q * C:(q + 1) * C, :].rearrange("c (e d) -> c e d", e=E),
                              cond_w.rearrange("e c d -> c e d")).then_inc(cond_loaded, 16)
            for e in range(X):
                act.dma_start(a_in[:, :, e * R:(e + 1) * R],
                              a[e].rearrange("(k p) r -> p k r", p=P)).then_inc(a_loaded, 16)

            def split_w(h):
                for k in range(KC):
                    act.wait_ge(w_turned, h * KC + k + 1)
                    nc.scalar.copy(w_hi[:, k, h * H:(h + 1) * H], turn_ps[(h * KC + k) % 3]).then_inc(w_hi_ready, 1)

            def split_x(t, j):
                return nc.scalar.copy(x_hi[:, j % 2, :], x_in[:, j % BODY, :])

            def split_y(j, h):
                nc.scalar.copy(y_hi[:, j // 2 % 2, h * HC:(h + 1) * HC, j % 2 * P:(j % 2 + 1) * P],
                               mix_ps[h][:, :].rearrange("p (k n) -> p k n", k=HC)).then_inc(y_hi_ready, 1)

            def make_mixer(t, j):
                for q in range(PER):
                    e = act.value_load(cond_ids[0:1, bass.ds(t * PER + q, 1)], min_val=0, max_val=E - 1)
                    part = slice(q * C, (q + 1) * C)
                    made = nc.scalar.copy(
                        mixer[part, j % 2, :, q * C:(q + 1) * C],
                        cond_all[part, bass.ds(e, 1), :, :].rearrange("p e s d -> p (e s) d").bitcast(fp32))
                made.then_inc(mixer_ready, 1)

            act.wait_ge(cond_loaded, 16 * PER)
            nc.scalar.copy(cond_all[:, :, 0, :], cond_in.rearrange("c (e d) -> c e d", e=E)).then_inc(cond_hi_ready, 1)
            split_w(0)
            act.wait_ge(ids_loaded, 16)
            act.wait_ge(cond_lo_ready, 1)
            act.wait_ge(mixer_zeroed, 1)
            for t in range(2):
                make_mixer(t, t)
                act.wait_ge(x_loaded[t], 16)
                split_x(t, t).then_inc(x_hi_ready, 1)
            act.wait_ge(a_loaded, 16 * X)
            nc.scalar.copy(a_hi[:, :, :], a_in).then_inc(a_hi_ready, 1)
            for t in range(2):
                for h in range(2):
                    act.wait_ge(mix_done, 2 * t + h + 1)
                    split_y(t, h)
            act.wait_ge(bm_scaled, 1)
            nc.scalar.copy(b_hi[:, :], bm_in[:, :]).then_inc(b_hi_ready, 1)
            act.wait_ge(x_loaded[2], 16)
            make_mixer(2, 2)
            split_x(2, 2).then_inc(x_hi_ready, 1)

            def step(i, first, last):
                for j in range(BODY):
                    t = i * BODY + j

                    def square_z(h):
                        cols = slice(h * H, (h + 1) * H)
                        act.wait_ge(z_b_ready, 2 * t + h + 1)
                        if not first or j + h >= 1:
                            act.wait_ge(m_squared, t + h)
                        nc.scalar.activation(squares[:, cols], z_b[:, j % 2, cols], ACT.Square,
                                             accum_out=z_sq[:, j % 2, h:h + 1]).then_inc(z_squared, 1)

                    if j % 2 == 0:
                        act.wait_ge(u_done, 2 * i + j // 2 + 1)
                        nc.scalar.copy(u_hi[:, :], u_ps[:, 0:2 * P]).then_inc(u_hi_ready, 1)
                    if not last or j + 2 < BODY:
                        act.wait_ge(mix_done, 2 * t + 5)
                        split_y(j + 2, 0)
                    if not first or j >= 2:
                        act.wait_ge(norm_z_ready, t - 1)
                    square_z(0)
                    if first and j == 0:
                        split_w(1)
                    if not last or j + 3 < BODY:
                        act.wait_ge(x_loaded[(j + 3) % BODY], 16 * (i + (j + 3) // BODY + 1))
                        act.wait_ge(mix_done, 2 * t + 4)
                        act.wait_ge(x_lo_ready, t + 2)
                        make_mixer(t + 3, j + 3)
                        split_x(t + 3, j + 3).then_inc(x_hi_ready, 1)
                    act.wait_ge(m_done, t + 1)
                    if not first or j >= 2:
                        act.wait_ge(norm_m_ready, t - 1)
                    act.wait_ge(z_squared, 2 * t + 1)
                    nc.scalar.activation(squares[:, :], m_ps[:, :], ACT.Square,
                                         accum_out=m_sq[:, j % 2:j % 2 + 1]).then_inc(m_squared, 1)
                    if not last or j + 2 < BODY:
                        act.wait_ge(mix_done, 2 * t + 6)
                        split_y(j + 2, 1)
                    square_z(1)

            steps(act, step)

        @block.vector
        def _(dve):
            def split_w(h):
                for k in range(KC):
                    dve.wait_ge(w_hi_ready, h * KC + k + 1)
                    cols = slice(h * H, (h + 1) * H)
                    nc.vector.tensor_tensor(w_lo[:, k, cols], turn_ps[(h * KC + k) % 3], w_hi[:, k, cols].bitcast(fp32),
                                            ALU.subtract).then_inc(w_lo_ready, 1)

            def split_y(j, h):
                part = (slice(None), j // 2 % 2, slice(h * HC, (h + 1) * HC), slice(j % 2 * P, (j % 2 + 1) * P))
                nc.vector.tensor_tensor(y_lo[part], mix_ps[h][:, :].rearrange("p (k n) -> p k n", k=HC),
                                        y_hi[part].bitcast(fp32), ALU.subtract).then_inc(y_lo_ready, 1)

            dve.wait_ge(cond_hi_ready, 1)
            nc.vector.tensor_tensor(cond_all[:, :, 1, :], cond_in.rearrange("c (e d) -> c e d", e=E),
                                    cond_all[:, :, 0, :].bitcast(fp32), ALU.subtract).then_inc(cond_lo_ready, 1)
            dve.wait_ge(bm_loaded, 16)
            dve.wait_ge(p_loaded, 16)
            nc.vector.tensor_scalar(bm_in[:, :], bm_in[:, :], p_col[:, 0:1], None, ALU.mult).then_inc(bm_scaled, 1)
            split_w(0)
            dve.wait_ge(a_hi_ready, 1)
            nc.vector.tensor_tensor(a_lo[:, :, :], a_in, a_hi[:, :, :].bitcast(fp32),
                                    ALU.subtract).then_inc(a_lo_ready, 1)
            for t in range(2):
                for h in range(2):
                    dve.wait_ge(y_hi_ready, 2 * t + h + 1)
                    split_y(t, h)
            dve.wait_ge(b_hi_ready, 1)
            nc.vector.tensor_tensor(b_lo[:, :], bm_in[:, :], b_hi[:, :].bitcast(fp32),
                                    ALU.subtract).then_inc(b_lo_ready, 1)
            dve.wait_ge(bias_loaded, 16)

            def step(i, first, last):
                for j in range(BODY):
                    t = i * BODY + j
                    one = slice(j % 2, j % 2 + 1)

                    def add_bias(h):
                        cols = slice(h * H, (h + 1) * H)
                        dve.wait_ge(z_done, 2 * t + h + 1)
                        if not first or j >= 2:
                            dve.wait_ge(z_squared, 2 * t + h - 3)
                            dve.wait_ge(residual_ready, 2 * t + h - 3)
                        nc.vector.tensor_tensor(z_b[:, j % 2, cols], z_ps[h][:, :], bias[:, cols],
                                                ALU.add).then_inc(z_b_ready, 1)

                    if j % 2 == 0:
                        dve.wait_ge(u_hi_ready, 2 * i + j // 2 + 1)
                        nc.vector.tensor_tensor(u_lo[:, :], u_ps[:, 0:2 * P], u_hi[:, :].bitcast(fp32),
                                                ALU.subtract).then_inc(u_lo_ready, 1)
                    if not last or j + 2 < BODY:
                        dve.wait_ge(y_hi_ready, 2 * t + 5)
                        split_y(j + 2, 0)
                    add_bias(0)
                    if first and j == 0:
                        split_w(1)
                    dve.wait_ge(norm_m_ready, t + 1)
                    nc.vector.tensor_scalar(twice_m[:, one], norm_m[:, one], EPS, 1.0 / CLAMP, ALU.add,
                                            ALU.mult).then_inc(twice_m_ready, 1)
                    dve.wait_ge(twice_m_ready, t + 1)
                    nc.vector.reciprocal(half_over_m[:, one], twice_m[:, one]).then_inc(over_m_ready, 1)
                    if not last or j + 2 < BODY:
                        dve.wait_ge(y_hi_ready, 2 * t + 6)
                        split_y(j + 2, 1)
                    add_bias(1)
                    dve.wait_ge(norm_z_ready, t + 1)
                    dve.wait_ge(over_m_ready, t + 1)
                    nc.vector.tensor_scalar(gamma[:, one], norm_z[:, one], half_over_m[:, one], 1.0, ALU.mult,
                                            ALU.min).then_inc(gamma_ready, 1)
                    dve.wait_ge(gamma_ready, t + 1)
                    dve.wait_ge(residual_ready, 2 * t + 2)
                    nc.vector.scalar_tensor_tensor(out=result[:, j % 2, :], in0=m_ps[:, :], scalar=gamma[:, one],
                                                   in1=result[:, j % 2, :], op0=ALU.mult,
                                                   op1=ALU.add).then_inc(out_ready, 1)

            steps(dve, step)

        @block.tensor
        def _(pe):
            def turn_w(h):
                source = w_early if h == 0 else w_late
                for k in range(KC):
                    n = h * KC + k
                    if n >= 3:
                        pe.wait_ge(w_lo_ready, n - 2)
                    for o in range(4):
                        if k == 0:
                            pe.wait_ge(w_loaded[h * 4 + o], 16)
                        turned = nc.tensor.transpose(turn_ps[n % 3][:, o * P:(o + 1) * P],
                                                     source[:, o, k * P:(k + 1) * P], ident[:, :])
                    turned.then_inc(w_turned, 1)

            def mix(j, h):
                for k in range(HC):
                    c = slice((h * HC + k) * P, (h * HC + k + 1) * P)
                    passes = [(x_hi[:, j % 2, c], mixer[:, j % 2, 0, :]), (x_hi[:, j % 2, c], mixer[:, j % 2, 1, :]),
                              (x_lo[:, j % 2, c], mixer[:, j % 2, 0, :])]
                    for n, (left, right) in enumerate(passes):
                        mixed = nc.tensor.matmul(mix_ps[h][:, k * P:(k + 1) * P], left, right,
                                                 start=(n == 0), stop=(n == len(passes) - 1))
                mixed.then_inc(mix_done, 1)

            def down(j):
                g = j // 2 % 2
                for k in range(KC):
                    passes = [(a_hi, y_hi), (a_hi, y_lo), (a_lo, y_hi)]
                    for n, (left, right) in enumerate(passes):
                        summed = nc.tensor.matmul(u_ps[:, 0:2 * P], left[:, k, :], right[:, g, k, :],
                                                  start=(k == 0 and n == 0), stop=(k == KC - 1 and n == 2))
                summed.then_inc(u_done, 1)

            def linear(j, h):
                g, r = j // 2 % 2, slice(j % 2 * P, (j % 2 + 1) * P)
                for k in range(KC):
                    passes = [(y_hi, w_hi), (y_hi, w_lo), (y_lo, w_hi)]
                    for n, (left, right) in enumerate(passes):
                        summed = nc.tensor.matmul(z_ps[h][:, :], left[:, g, k, r], right[:, k, h * H:(h + 1) * H],
                                                  start=(k == 0 and n == 0), stop=(k == KC - 1 and n == 2))
                summed.then_inc(z_done, 1)

            def up(j):
                r = slice(j % 2 * P, (j % 2 + 1) * P)
                passes = [(u_hi, b_hi), (u_hi, b_lo), (u_lo, b_hi)]
                for n, (left, right) in enumerate(passes):
                    for h in range(2):
                        c = slice(h * H, (h + 1) * H)
                        summed = nc.tensor.matmul(m_ps[:, c], left[:, r], right[:, c], start=(n == 0), stop=(n == 2))
                summed.then_inc(m_done, 1)

            pe.wait_ge(ident_set, 1)
            turn_w(0)
            for t in range(2):
                pe.wait_ge(mixer_ready, t + 1)
                pe.wait_ge(x_hi_ready, t + 1)
                pe.wait_ge(x_lo_ready, t + 1)
                for h in range(2):
                    if t >= 1:
                        pe.wait_ge(y_lo_ready, 2 * t + h - 1)
                    mix(t, h)

            def step(i, first, last):
                for j in range(BODY):
                    t = i * BODY + j

                    if j % 2 == 0:
                        pe.wait_ge(y_hi_ready, 2 * t + 4)
                        pe.wait_ge(y_lo_ready, 2 * t + 4)
                        if first and j == 0:
                            pe.wait_ge(a_hi_ready, 1)
                            pe.wait_ge(a_lo_ready, 1)
                        else:
                            pe.wait_ge(u_lo_ready, 2 * i + j // 2)
                        down(j)
                    if not last or j + 2 < BODY:
                        pe.wait_ge(mixer_ready, t + 3)
                        pe.wait_ge(x_hi_ready, t + 3)
                        pe.wait_ge(x_lo_ready, t + 3)
                        pe.wait_ge(y_lo_ready, 2 * t + 3)
                        mix(j + 2, 0)
                    if first and j == 0:
                        pe.wait_ge(w_hi_ready, KC)
                        pe.wait_ge(w_lo_ready, KC)
                    else:
                        pe.wait_ge(z_b_ready, 2 * t - 1)
                    linear(j, 0)
                    if first and j == 0:
                        turn_w(1)
                        pe.wait_ge(b_hi_ready, 1)
                        pe.wait_ge(b_lo_ready, 1)
                        pe.wait_ge(w_hi_ready, 2 * KC)
                        pe.wait_ge(w_lo_ready, 2 * KC)
                    pe.wait_ge(u_hi_ready, 2 * i + j // 2 + 1)
                    pe.wait_ge(u_lo_ready, 2 * i + j // 2 + 1)
                    if not first or j >= 1:
                        pe.wait_ge(out_ready, t)
                    up(j)
                    if not last or j + 2 < BODY:
                        pe.wait_ge(y_lo_ready, 2 * t + 4)
                        mix(j + 2, 1)
                    if not first or j >= 1:
                        pe.wait_ge(z_b_ready, 2 * t)
                    linear(j, 1)

            steps(pe, step)


_INS = ['x', 'itok_B_0_15', 'L0_cond_weights', 'L0_ffn_W', 'L0_ffn_b', 'L0_ffn_A', 'L0_ffn_B', 'L0_ffn_p_scores']


def kernel(**inputs):
    import numpy as _np
    import concourse.bacc as _bacc
    from concourse import mybir as _mybir
    from concourse.bass_utils import run_bass_kernel_spmd as _run

    nc = _bacc.Bacc("TRN2", target_bir_lowering=False, num_devices=1)
    arrays, args = {}, []
    for name in _INS:
        a = _np.ascontiguousarray(inputs[name])
        arrays[f"in_{name}_dram"] = a
        args.append(nc.dram_tensor(f"in_{name}_dram", a.shape, _mybir.dt.from_np(a.dtype), kind="ExternalInput").ap())
    shape = inputs['x'].shape
    args.append(nc.dram_tensor("out_0_dram", shape, _mybir.dt.float32, kind="ExternalOutput").ap())
    conditioned_clamped_low_rank_linear_kernel(nc, *args)
    r = _run(nc, [arrays], core_ids=[0])
    return r.results[0]["out_0_dram"]
```

```python
import concourse.bass as bass
from concourse import mybir
from contextlib import ExitStack


def conditioned_clamped_low_rank_linear_kernel(
    nc: bass.Bass,
    x: bass.AP,
    condition: bass.AP,
    cond_w: bass.AP,
    w: bass.AP,
    b: bass.AP,
    a: bass.AP,
    bm: bass.AP,
    p_scores: bass.AP,
    out: bass.AP,
):
    fp32 = mybir.dt.float32
    fp32r = mybir.dt.float32r
    bf16 = mybir.dt.bfloat16
    i32 = mybir.dt.int32
    ALU = mybir.AluOpType
    ACT = mybir.ActivationFunctionType

    B, C, D = x.shape
    E = cond_w.shape[0]
    X, _, R = a.shape
    P = 128
    PER = P // C
    TILES = B // PER
    KC = D // P
    HC = KC // 2
    H = D // 2
    XR = X * R
    NW = D // P
    BODY = 4
    STEPS = TILES // BODY
    CLAMP, EPS = 0.5, 1e-6
    assert (C * PER, XR, H, D % P, TILES % BODY) == (P, P, 512, 0, 0) and STEPS >= 3

    x_tiles = x.rearrange("(n q) c t -> n (q c) t", q=PER)
    out_tiles = out.rearrange("(n q) c t -> n (q c) t", q=PER)

    ctx = ExitStack()
    with ctx:
        def sb(name, shape, dt):
            return ctx.enter_context(nc.sbuf_tensor(name, shape, dt))

        def pb(name, shape):
            return ctx.enter_context(nc.psum_tensor(name, shape, fp32))

        def sem(name):
            return ctx.enter_context(nc.semaphore(name))

        w_hi = sb("w_hi", [P, KC, D], fp32r)
        w_lo = sb("w_lo", [P, KC, D], fp32r)
        a_hi = sb("a_hi", [P, KC, XR], fp32r)
        a_lo = sb("a_lo", [P, KC, XR], fp32r)
        b_hi = sb("b_hi", [P, D], fp32r)
        b_lo = sb("b_lo", [P, D], fp32r)
        cond_all = sb("cond_all", [P, E, C], fp32)
        mixer = sb("mixer", [P, 2, P], fp32)
        bias = sb("bias", [P, D], fp32)
        cond_ids = sb("cond_ids", [1, B], i32)
        p_col = sb("p_col", [P, 1], fp32)
        ident = sb("ident", [P, P], fp32)

        x_in = sb("x_in", [P, BODY, D], fp32)
        y_hi = sb("y_hi", [P, 2, KC, 2 * P], fp32r)
        y_lo = sb("y_lo", [P, 2, KC, 2 * P], fp32r)
        u_hi = sb("u_hi", [P, 2 * P], fp32r)
        u_lo = sb("u_lo", [P, 2 * P], fp32r)
        rows = sb("rows", [P, 4, D], fp32)
        w_late = sb("w_late", [P, 4, D], fp32)
        bm_in = sb("bm_in", [P, D], fp32)
        a_in = sb("a_in", [P, KC, XR], fp32)
        squares = sb("squares", [P, D], bf16)
        z_sq = sb("z_sq", [P, 2, 2], fp32)
        z_sum = sb("z_sum", [P, 2], fp32)
        half = sb("half", [P, 1], fp32)
        m_sq = sb("m_sq", [P, 2], fp32)
        norm_z = sb("norm_z", [P, 2], fp32)
        norm_m = sb("norm_m", [P, 2], fp32)
        twice_m = sb("twice_m", [P, 2], fp32)
        half_over_m = sb("half_over_m", [P, 2], fp32)
        gamma = sb("gamma", [P, 2], fp32)

        z_b = rows[:, 0:2, :]
        result = rows[:, 2:4, :]
        w_early = rows[:, :, :]

        mix_ps = [pb(f"mix_ps{h}", [P, H]) for h in range(2)]
        z_ps = [pb(f"z_ps{h}", [P, H]) for h in range(2)]
        m_ps = pb("m_ps", [P, 2 * H])
        u_ps = pb("u_ps", [P, H])
        turn_ps = [z_ps[1][:, :], m_ps[:, 0:H], m_ps[:, H:2 * H], u_ps[:, :]]
        TURNS = len(turn_ps)

        x_loaded = [sem(f"x_loaded{s}") for s in range(BODY)]
        out_stored = [sem(f"out_stored{s}") for s in range(2)]
        w_loaded = [sem(f"w_loaded{n}") for n in range(8)]
        ids_loaded = sem("ids_loaded")
        cond_loaded = sem("cond_loaded")
        a_loaded = sem("a_loaded")
        bm_loaded = sem("bm_loaded")
        p_loaded = sem("p_loaded")
        bias_loaded = sem("bias_loaded")
        ones_set = sem("ones_set")
        ident_set = sem("ident_set")
        half_set = sem("half_set")
        mixer_zeroed = sem("mixer_zeroed")
        w_turned = sem("w_turned")
        w_hi_ready = sem("w_hi_ready")
        w_lo_ready = sem("w_lo_ready")
        a_hi_ready = sem("a_hi_ready")
        a_lo_ready = sem("a_lo_ready")
        bm_scaled = sem("bm_scaled")
        b_hi_ready = sem("b_hi_ready")
        b_lo_ready = sem("b_lo_ready")
        mixer_ready = sem("mixer_ready")
        mix_done = sem("mix_done")
        y_hi_ready = sem("y_hi_ready")
        y_lo_ready = sem("y_lo_ready")
        u_done = sem("u_done")
        u_hi_ready = sem("u_hi_ready")
        u_lo_ready = sem("u_lo_ready")
        z_done = sem("z_done")
        z_b_ready = sem("z_b_ready")
        z_squared = sem("z_squared")
        m_done = sem("m_done")
        m_squared = sem("m_squared")
        norm_m_ready = sem("norm_m_ready")
        norm_z_ready = sem("norm_z_ready")
        z_sum_ready = sem("z_sum_ready")
        residual_ready = sem("residual_ready")
        twice_m_ready = sem("twice_m_ready")
        over_m_ready = sem("over_m_ready")
        gamma_ready = sem("gamma_ready")
        out_ready = sem("out_ready")

        def steps(engine, step):
            step(0, True, False)
            with engine.Fori(1, STEPS - 1) as i:
                step(i, False, False)
            step(STEPS - 1, False, True)

        block = ctx.enter_context(nc.Block())

        @block.sync
        def _(sp):
            sp.dma_start(cond_ids[:, :], condition.rearrange("(o n) -> o n", o=1)).then_inc(ids_loaded, 16)
            for q in range(PER):
                sp.dma_start(cond_all[q * C:(q + 1) * C, :, :], cond_w.rearrange("e c d -> c e d")).then_inc(cond_loaded, 16)
            sp.dma_start(x_in[:, 0, :], x_tiles[0]).then_inc(x_loaded[0], 16)
            for n in range(4):
                sp.dma_start(w_early[:, n, :], w[n * P:(n + 1) * P, :]).then_inc(w_loaded[n], 16)
            for n in range(4):
                sp.dma_start(w_late[:, n, :], w[(n + 4) * P:(n + 5) * P, :]).then_inc(w_loaded[4 + n], 16)
            sp.dma_start(x_in[:, 1, :], x_tiles[1]).then_inc(x_loaded[1], 16)
            for e in range(X):
                sp.dma_start(a_in[:, :, e * R:(e + 1) * R], a[e].rearrange("(k p) r -> p k r", p=P)).then_inc(a_loaded, 16)
            sp.dma_start(p_col[:, :], p_scores.rearrange("(e o) -> e o", o=1).unsqueeze(1)
                         .to_broadcast([X, R, 1])).then_inc(p_loaded, 16)
            sp.dma_start(bm_in[:, :], bm.rearrange("e r o -> (e r) o")).then_inc(bm_loaded, 16)
            sp.dma_start(bias[:, :], b.rearrange("(o n) -> o n", o=1).to_broadcast([P, D])).then_inc(bias_loaded, 16)
            for t in range(2, BODY):
                sp.dma_start(x_in[:, t, :], x_tiles[t]).then_inc(x_loaded[t], 16)

            def step(i, first, last):
                for j in range(BODY):
                    t = i * BODY + j
                    if not last:
                        sp.wait_ge(residual_ready, 2 * t + 2)
                        sp.dma_start(x_in[:, j, :], x_tiles[t + BODY]).then_inc(x_loaded[j], 16)
                    sp.wait_ge(out_ready, t + 1)
                    sp.dma_start(out_tiles[t], result[:, j % 2, :]).then_inc(out_stored[j % 2], 16)

            steps(sp, step)
            for s in range(2):
                sp.wait_ge(out_stored[s], 16 * (TILES // 2))

        @block.gpsimd
        def _(pool):
            nc.gpsimd.memset(ident[:, :], 1.0).then_inc(ones_set, 1)
            pool.wait_ge(ones_set, 1)
            nc.gpsimd.affine_select(out=ident[:, :], in_=ident[:, :], pattern=[[-1, P]], compare_op=ALU.is_equal,
                                    fill=0.0, base=0, channel_multiplier=1).then_inc(ident_set, 1)
            nc.gpsimd.memset(half[:, :], 0.5).then_inc(half_set, 1)
            nc.gpsimd.memset(mixer[:, :, :], 0.0).then_inc(mixer_zeroed, 1)

            pool.wait_ge(half_set, 1)

            def step(i, first, last):
                for j in range(BODY):
                    t = i * BODY + j
                    one = slice(j % 2, j % 2 + 1)

                    def residual(h):
                        cols = slice(h * H, (h + 1) * H)
                        pool.wait_ge(z_b_ready, 2 * t + h + 1)
                        nc.gpsimd.tensor_tensor(result[:, j % 2, cols], z_b[:, j % 2, cols], x_in[:, j, cols],
                                                ALU.add).then_inc(residual_ready, 1)

                    if not first or j >= 2:
                        pool.wait_ge(out_stored[j % 2], 16 * (2 * i + j // 2))
                    residual(0)
                    pool.wait_ge(m_squared, t + 1)
                    nc.gpsimd.tensor_tensor(norm_m[:, one], m_sq[:, one], half[:, :], ALU.pow).then_inc(norm_m_ready, 1)
                    residual(1)
                    pool.wait_ge(z_squared, 2 * t + 2)
                    nc.gpsimd.tensor_tensor(z_sum[:, one], z_sq[:, j % 2, 0:1], z_sq[:, j % 2, 1:2],
                                            ALU.add).then_inc(z_sum_ready, 1)
                    pool.wait_ge(z_sum_ready, t + 1)
                    nc.gpsimd.tensor_tensor(norm_z[:, one], z_sum[:, one], half[:, :], ALU.pow).then_inc(norm_z_ready, 1)

            steps(pool, step)

        @block.scalar
        def _(act):
            def split_w(n):
                for c in range(2):
                    act.wait_ge(w_turned, 2 * n + c + 1)
                    nc.scalar.copy(w_hi[:, c * HC:(c + 1) * HC, n * P:(n + 1) * P],
                                   turn_ps[(2 * n + c) % TURNS].rearrange("p (k n) -> p k n", k=HC)
                                   ).then_inc(w_hi_ready, 1)

            def split_y(j, h):
                nc.scalar.copy(y_hi[:, j // 2 % 2, h * HC:(h + 1) * HC, j % 2 * P:(j % 2 + 1) * P],
                               mix_ps[h][:, :].rearrange("p (k n) -> p k n", k=HC)).then_inc(y_hi_ready, 1)

            def make_mixer(t, j):
                for q in range(PER):
                    e = act.value_load(cond_ids[0:1, bass.ds(t * PER + q, 1)], min_val=0, max_val=E - 1)
                    part = slice(q * C, (q + 1) * C)
                    made = nc.scalar.copy(mixer[part, j % 2, q * C:(q + 1) * C],
                                          cond_all[part, bass.ds(e, 1), :].rearrange("p e d -> p (e d)"))
                made.then_inc(mixer_ready, 1)

            act.wait_ge(ids_loaded, 16)
            act.wait_ge(cond_loaded, 16 * PER)
            act.wait_ge(mixer_zeroed, 1)
            for t in range(2):
                make_mixer(t, t)
            for h in range(2):
                act.wait_ge(mix_done, h + 1)
                split_y(0, h)
            make_mixer(2, 2)
            for n in range(NW):
                split_w(n)
            for h in range(2):
                act.wait_ge(mix_done, h + 3)
                split_y(1, h)
            act.wait_ge(a_loaded, 16 * X)
            nc.scalar.copy(a_hi[:, :, :], a_in[:, :, :]).then_inc(a_hi_ready, 1)
            act.wait_ge(bm_scaled, 1)
            nc.scalar.copy(b_hi[:, :], bm_in[:, :]).then_inc(b_hi_ready, 1)

            def step(i, first, last):
                for j in range(BODY):
                    t = i * BODY + j

                    def square_z(h):
                        cols = slice(h * H, (h + 1) * H)
                        act.wait_ge(z_b_ready, 2 * t + h + 1)
                        if not first or j + h >= 1:
                            act.wait_ge(m_squared, t + h)
                        nc.scalar.activation(squares[:, cols], z_b[:, j % 2, cols], ACT.Square,
                                             accum_out=z_sq[:, j % 2, h:h + 1]).then_inc(z_squared, 1)

                    if j % 2 == 0:
                        act.wait_ge(u_done, 2 * i + j // 2 + 1)
                        nc.scalar.copy(u_hi[:, :], u_ps[:, 0:2 * P]).then_inc(u_hi_ready, 1)
                    if not last or j + 2 < BODY:
                        act.wait_ge(mix_done, 2 * t + 5)
                        split_y(j + 2, 0)
                    if not first or j >= 2:
                        act.wait_ge(norm_z_ready, t - 1)
                    square_z(0)
                    if not last or j + 3 < BODY:
                        act.wait_ge(mix_done, 2 * t + 4)
                        make_mixer(t + 3, j + 3)
                    act.wait_ge(m_done, t + 1)
                    if not first or j >= 2:
                        act.wait_ge(norm_m_ready, t - 1)
                    act.wait_ge(z_squared, 2 * t + 1)
                    nc.scalar.activation(squares[:, :], m_ps[:, :], ACT.Square,
                                         accum_out=m_sq[:, j % 2:j % 2 + 1]).then_inc(m_squared, 1)
                    if not last or j + 2 < BODY:
                        act.wait_ge(mix_done, 2 * t + 6)
                        split_y(j + 2, 1)
                    square_z(1)

            steps(act, step)

        @block.vector
        def _(dve):
            def split_w(n):
                for c in range(2):
                    part = (slice(None), slice(c * HC, (c + 1) * HC), slice(n * P, (n + 1) * P))
                    dve.wait_ge(w_hi_ready, 2 * n + c + 1)
                    nc.vector.tensor_tensor(w_lo[part], turn_ps[(2 * n + c) % TURNS].rearrange("p (k n) -> p k n", k=HC),
                                            w_hi[part].bitcast(fp32), ALU.subtract).then_inc(w_lo_ready, 1)

            def split_y(j, h):
                part = (slice(None), j // 2 % 2, slice(h * HC, (h + 1) * HC), slice(j % 2 * P, (j % 2 + 1) * P))
                nc.vector.tensor_tensor(y_lo[part], mix_ps[h][:, :].rearrange("p (k n) -> p k n", k=HC),
                                        y_hi[part].bitcast(fp32), ALU.subtract).then_inc(y_lo_ready, 1)

            for h in range(2):
                dve.wait_ge(y_hi_ready, h + 1)
                split_y(0, h)
            for n in range(NW):
                split_w(n)
            for h in range(2):
                dve.wait_ge(y_hi_ready, h + 3)
                split_y(1, h)
            dve.wait_ge(a_hi_ready, 1)
            nc.vector.tensor_tensor(a_lo[:, :, :], a_in[:, :, :], a_hi[:, :, :].bitcast(fp32),
                                    ALU.subtract).then_inc(a_lo_ready, 1)
            dve.wait_ge(bm_loaded, 16)
            dve.wait_ge(p_loaded, 16)
            nc.vector.tensor_scalar(bm_in[:, :], bm_in[:, :], p_col[:, 0:1], None, ALU.mult).then_inc(bm_scaled, 1)
            dve.wait_ge(b_hi_ready, 1)
            nc.vector.tensor_tensor(b_lo[:, :], bm_in[:, :], b_hi[:, :].bitcast(fp32),
                                    ALU.subtract).then_inc(b_lo_ready, 1)
            dve.wait_ge(bias_loaded, 16)

            def step(i, first, last):
                for j in range(BODY):
                    t = i * BODY + j
                    one = slice(j % 2, j % 2 + 1)

                    def add_bias(h):
                        cols = slice(h * H, (h + 1) * H)
                        dve.wait_ge(z_done, 2 * t + h + 1)
                        if not first or j >= 2:
                            dve.wait_ge(z_squared, 2 * t + h - 3)
                            dve.wait_ge(residual_ready, 2 * t + h - 3)
                        nc.vector.tensor_tensor(z_b[:, j % 2, cols], z_ps[h][:, :], bias[:, cols],
                                                ALU.add).then_inc(z_b_ready, 1)

                    if j % 2 == 0:
                        dve.wait_ge(u_hi_ready, 2 * i + j // 2 + 1)
                        nc.vector.tensor_tensor(u_lo[:, :], u_ps[:, 0:2 * P], u_hi[:, :].bitcast(fp32),
                                                ALU.subtract).then_inc(u_lo_ready, 1)
                    if not last or j + 2 < BODY:
                        dve.wait_ge(y_hi_ready, 2 * t + 5)
                        split_y(j + 2, 0)
                    add_bias(0)
                    if not last or j + 2 < BODY:
                        dve.wait_ge(y_hi_ready, 2 * t + 6)
                        split_y(j + 2, 1)
                    dve.wait_ge(norm_m_ready, t + 1)
                    nc.vector.tensor_scalar(twice_m[:, one], norm_m[:, one], EPS, 1.0 / CLAMP, ALU.add,
                                            ALU.mult).then_inc(twice_m_ready, 1)
                    dve.wait_ge(twice_m_ready, t + 1)
                    nc.vector.reciprocal(half_over_m[:, one], twice_m[:, one]).then_inc(over_m_ready, 1)
                    add_bias(1)
                    dve.wait_ge(norm_z_ready, t + 1)
                    dve.wait_ge(over_m_ready, t + 1)
                    nc.vector.tensor_scalar(gamma[:, one], norm_z[:, one], half_over_m[:, one], 1.0, ALU.mult,
                                            ALU.min).then_inc(gamma_ready, 1)
                    dve.wait_ge(gamma_ready, t + 1)
                    dve.wait_ge(residual_ready, 2 * t + 2)
                    nc.vector.scalar_tensor_tensor(out=result[:, j % 2, :], in0=m_ps[:, :], scalar=gamma[:, one],
                                                   in1=result[:, j % 2, :], op0=ALU.mult,
                                                   op1=ALU.add).then_inc(out_ready, 1)

            steps(dve, step)

        @block.tensor
        def _(pe):
            def turn_w(n, c):
                source = w_early if n < 4 else w_late
                at = 2 * n + c
                if at >= TURNS:
                    pe.wait_ge(w_lo_ready, at - TURNS + 1)
                if c == 0:
                    pe.wait_ge(w_loaded[n], 16)
                for k in range(HC):
                    turned = nc.tensor.transpose(turn_ps[at % TURNS][:, k * P:(k + 1) * P],
                                                 source[:, n % 4, (c * HC + k) * P:(c * HC + k + 1) * P], ident[:, :])
                turned.then_inc(w_turned, 1)

            def mix(j, h):
                for k in range(HC):
                    mixed = nc.tensor.matmul(mix_ps[h][:, k * P:(k + 1) * P],
                                             x_in[:, j % BODY, (h * HC + k) * P:(h * HC + k + 1) * P],
                                             mixer[:, j % 2, :], start=True, stop=True)
                mixed.then_inc(mix_done, 1)

            def down(j):
                g = j // 2 % 2
                for k in range(KC):
                    passes = [(a_hi, y_hi), (a_hi, y_lo), (a_lo, y_hi)]
                    for n, (left, right) in enumerate(passes):
                        summed = nc.tensor.matmul(u_ps[:, 0:2 * P], left[:, k, :], right[:, g, k, :],
                                                  start=(k == 0 and n == 0), stop=(k == KC - 1 and n == 2))
                summed.then_inc(u_done, 1)

            def linear(j, h, after_chunk=None):
                g, r = j // 2 % 2, slice(j % 2 * P, (j % 2 + 1) * P)
                for k in range(KC):
                    passes = [(y_hi, w_hi), (y_hi, w_lo), (y_lo, w_hi)]
                    for n, (left, right) in enumerate(passes):
                        summed = nc.tensor.matmul(z_ps[h][:, :], left[:, g, k, r], right[:, k, h * H:(h + 1) * H],
                                                  start=(k == 0 and n == 0), stop=(k == KC - 1 and n == 2))
                    if after_chunk is not None:
                        after_chunk(k)
                summed.then_inc(z_done, 1)

            def up(j):
                r = slice(j % 2 * P, (j % 2 + 1) * P)
                passes = [(u_hi, b_hi), (u_hi, b_lo), (u_lo, b_hi)]
                for n, (left, right) in enumerate(passes):
                    for h in range(2):
                        c = slice(h * H, (h + 1) * H)
                        summed = nc.tensor.matmul(m_ps[:, c], left[:, r], right[:, c], start=(n == 0), stop=(n == 2))
                summed.then_inc(m_done, 1)

            pe.wait_ge(x_loaded[0], 16)
            pe.wait_ge(mixer_ready, 1)
            for h in range(2):
                mix(0, h)
            pe.wait_ge(ident_set, 1)
            for n in range(NW // 2):
                for c in range(2):
                    turn_w(n, c)
            pe.wait_ge(y_hi_ready, 2)
            pe.wait_ge(y_lo_ready, 2)
            pe.wait_ge(w_hi_ready, NW)
            pe.wait_ge(w_lo_ready, NW)
            linear(0, 0, after_chunk=lambda k: turn_w(NW // 2 + k // 2, k % 2))
            pe.wait_ge(x_loaded[1], 16)
            pe.wait_ge(mixer_ready, 2)
            for h in range(2):
                mix(1, h)

            def step(i, first, last):
                for j in range(BODY):
                    t = i * BODY + j

                    if j % 2 == 0:
                        pe.wait_ge(y_hi_ready, 2 * t + 4)
                        pe.wait_ge(y_lo_ready, 2 * t + 4)
                        if first and j == 0:
                            pe.wait_ge(a_hi_ready, 1)
                            pe.wait_ge(a_lo_ready, 1)
                        else:
                            pe.wait_ge(u_lo_ready, 2 * i + j // 2)
                        down(j)
                    if not last or j + 2 < BODY:
                        pe.wait_ge(x_loaded[(j + 2) % BODY], 16 * (i + (j + 2) // BODY + 1))
                        pe.wait_ge(mixer_ready, t + 3)
                        pe.wait_ge(y_lo_ready, 2 * t + 3)
                        mix(j + 2, 0)
                    if not first or j >= 1:
                        pe.wait_ge(z_b_ready, 2 * t - 1)
                        linear(j, 0)
                    else:
                        pe.wait_ge(b_hi_ready, 1)
                        pe.wait_ge(b_lo_ready, 1)
                    pe.wait_ge(u_hi_ready, 2 * i + j // 2 + 1)
                    pe.wait_ge(u_lo_ready, 2 * i + j // 2 + 1)
                    if not first or j >= 1:
                        pe.wait_ge(out_ready, t)
                    up(j)
                    if not last or j + 2 < BODY:
                        pe.wait_ge(y_lo_ready, 2 * t + 4)
                        mix(j + 2, 1)
                    if not first or j >= 1:
                        pe.wait_ge(z_b_ready, 2 * t)
                    else:
                        pe.wait_ge(w_hi_ready, 2 * NW)
                        pe.wait_ge(w_lo_ready, 2 * NW)
                    linear(j, 1)

            steps(pe, step)


_INS = ['x', 'itok_B_0_15', 'L0_cond_weights', 'L0_ffn_W', 'L0_ffn_b', 'L0_ffn_A', 'L0_ffn_B', 'L0_ffn_p_scores']


def kernel(**inputs):
    import numpy as _np
    import concourse.bacc as _bacc
    from concourse import mybir as _mybir
    from concourse.bass_utils import run_bass_kernel_spmd as _run

    nc = _bacc.Bacc("TRN2", target_bir_lowering=False, num_devices=1)
    arrays, args = {}, []
    for name in _INS:
        a = _np.ascontiguousarray(inputs[name])
        arrays[f"in_{name}_dram"] = a
        args.append(nc.dram_tensor(f"in_{name}_dram", a.shape, _mybir.dt.from_np(a.dtype), kind="ExternalInput").ap())
    shape = inputs['x'].shape
    args.append(nc.dram_tensor("out_0_dram", shape, _mybir.dt.float32, kind="ExternalOutput").ap())
    conditioned_clamped_low_rank_linear_kernel(nc, *args)
    r = _run(nc, [arrays], core_ids=[0])
    return r.results[0]["out_0_dram"]
```

```python
import concourse.bass as bass
from concourse import mybir
from contextlib import ExitStack


def conditioned_clamped_low_rank_linear_kernel(
    nc: bass.Bass,
    x: bass.AP,
    condition: bass.AP,
    cond_w: bass.AP,
    w: bass.AP,
    b: bass.AP,
    a: bass.AP,
    bm: bass.AP,
    p_scores: bass.AP,
    out: bass.AP,
):
    fp32 = mybir.dt.float32
    fp32r = mybir.dt.float32r
    bf16 = mybir.dt.bfloat16
    i32 = mybir.dt.int32
    ALU = mybir.AluOpType
    ACT = mybir.ActivationFunctionType

    B, C, D = x.shape
    E = cond_w.shape[1]
    _, X, R = a.shape
    P = 128
    PER = P // C
    TILES = B // PER
    KC = D // P
    HC = KC // 2
    H = D // 2
    XR = X * R
    WARM = 12
    MIX_1_AFTER = 4
    BODY = 4
    STEPS = TILES // BODY
    CLAMP, EPS = 0.5, 1e-6
    assert (C * PER, XR, H, D % P, TILES % BODY) == (P, P, 512, 0, 0) and STEPS >= 3

    x_tiles = x.rearrange("(n q) c t -> n (q c) t", q=PER)
    out_tiles = out.rearrange("(n q) c t -> n (q c) t", q=PER)

    ctx = ExitStack()
    with ctx:
        def sb(name, shape, dt):
            return ctx.enter_context(nc.sbuf_tensor(name, shape, dt))

        def pb(name, shape):
            return ctx.enter_context(nc.psum_tensor(name, shape, fp32))

        def sem(name):
            return ctx.enter_context(nc.semaphore(name))

        w_hi = sb("w_hi", [P, KC, D], fp32r)
        w_lo = sb("w_lo", [P, KC, D], fp32r)
        a_hi = sb("a_hi", [P, KC, XR], fp32r)
        a_lo = sb("a_lo", [P, KC, XR], fp32r)
        b_hi = sb("b_hi", [P, D], fp32r)
        b_lo = sb("b_lo", [P, D], fp32r)
        cond_all = sb("cond_all", [P, E, C], fp32)
        mixer = sb("mixer", [P, 2, P], fp32)
        bias = sb("bias", [P, D], fp32)
        cond_ids = sb("cond_ids", [1, B], i32)
        p_col = sb("p_col", [P, 1], fp32)
        idle = sb("idle", [P, H], bf16)

        x_in = sb("x_in", [P, BODY, D], fp32)
        y_hi = sb("y_hi", [P, 2, KC, 2 * P], fp32r)
        y_lo = sb("y_lo", [P, 2, KC, 2 * P], fp32r)
        u_hi = sb("u_hi", [P, 2 * P], fp32r)
        u_lo = sb("u_lo", [P, 2 * P], fp32r)
        rows = sb("rows", [P, 4, D], fp32)
        w_late = sb("w_late", [P, KC - 4, D], fp32)
        bm_in = sb("bm_in", [P, D], fp32)
        a_in = sb("a_in", [P, KC, XR], fp32)
        squares = sb("squares", [P, D], bf16)
        z_sq = sb("z_sq", [P, 2, 2], fp32)
        z_sum = sb("z_sum", [P, 2], fp32)
        half = sb("half", [P, 1], fp32)
        m_sq = sb("m_sq", [P, 2], fp32)
        norm_z = sb("norm_z", [P, 2], fp32)
        norm_m = sb("norm_m", [P, 2], fp32)
        twice_m = sb("twice_m", [P, 2], fp32)
        half_over_m = sb("half_over_m", [P, 2], fp32)
        gamma = sb("gamma", [P, 2], fp32)

        z_b = rows[:, 0:2, :]
        result = rows[:, 2:4, :]
        w_in = [rows[:, k, :] if k < 4 else w_late[:, k - 4, :] for k in range(KC)]

        mix_ps = [pb(f"mix_ps{h}", [P, H]) for h in range(2)]
        z_ps = [pb(f"z_ps{h}", [P, H]) for h in range(2)]
        m_ps = pb("m_ps", [P, 2 * H])
        u_ps = pb("u_ps", [P, H])

        x_loaded = [sem(f"x_loaded{s}") for s in range(BODY)]
        out_stored = [sem(f"out_stored{s}") for s in range(2)]
        w_loaded = [sem(f"w_loaded{k}") for k in range(KC)]
        ids_loaded = sem("ids_loaded")
        cond_loaded = sem("cond_loaded")
        a_loaded = sem("a_loaded")
        bm_loaded = sem("bm_loaded")
        p_loaded = sem("p_loaded")
        bias_loaded = sem("bias_loaded")
        idle_set = sem("idle_set")
        table_loaded = sem("table_loaded")
        half_set = sem("half_set")
        mixer_zeroed = sem("mixer_zeroed")
        w_hi_ready = sem("w_hi_ready")
        w_lo_ready = sem("w_lo_ready")
        a_hi_ready = sem("a_hi_ready")
        a_lo_ready = sem("a_lo_ready")
        bm_scaled = sem("bm_scaled")
        b_hi_ready = sem("b_hi_ready")
        b_lo_ready = sem("b_lo_ready")
        mixer_ready = sem("mixer_ready")
        mix_done = sem("mix_done")
        y_hi_ready = sem("y_hi_ready")
        y_lo_ready = sem("y_lo_ready")
        u_done = sem("u_done")
        u_hi_ready = sem("u_hi_ready")
        u_lo_ready = sem("u_lo_ready")
        z_done = sem("z_done")
        z_b_ready = sem("z_b_ready")
        z_squared = sem("z_squared")
        m_done = sem("m_done")
        m_squared = sem("m_squared")
        norm_m_ready = sem("norm_m_ready")
        norm_z_ready = sem("norm_z_ready")
        z_sum_ready = sem("z_sum_ready")
        residual_0_ready = sem("residual_0_ready")
        residual_1_ready = sem("residual_1_ready")
        twice_m_ready = sem("twice_m_ready")
        over_m_ready = sem("over_m_ready")
        gamma_ready = sem("gamma_ready")
        out_ready = sem("out_ready")

        def steps(engine, step):
            step(0, True, False)
            with engine.Fori(1, STEPS - 1) as i:
                step(i, False, False)
            step(STEPS - 1, False, True)

        block = ctx.enter_context(nc.Block())

        @block.sync
        def _(sp):
            sp.dma_start(cond_ids[:, :], condition.rearrange("(o n) -> o n", o=1)).then_inc(ids_loaded, 16)
            for q in range(PER):
                sp.dma_start(cond_all[q * C:(q + 1) * C, :, :], cond_w).then_inc(cond_loaded, 16)
            sp.dma_start(x_in[:, 0, :], x_tiles[0]).then_inc(x_loaded[0], 16)
            for k in range(KC):
                sp.dma_start(w_in[k], w[k * P:(k + 1) * P, :]).then_inc(w_loaded[k], 16)
                if k == MIX_1_AFTER:
                    sp.dma_start(x_in[:, 1, :], x_tiles[1]).then_inc(x_loaded[1], 16)
            sp.dma_start(x_in[:, 2, :], x_tiles[2]).then_inc(x_loaded[2], 16)
            sp.dma_start(a_in[:, :, :], a.rearrange("(k p) e r -> p k (e r)", p=P)).then_inc(a_loaded, 16)
            sp.dma_start(p_col[:, :], p_scores.rearrange("(e o) -> e o", o=1).unsqueeze(1)
                         .to_broadcast([X, R, 1])).then_inc(p_loaded, 16)
            sp.dma_start(bm_in[:, :], bm.rearrange("e r o -> (e r) o")).then_inc(bm_loaded, 16)
            sp.dma_start(bias[:, :], b.rearrange("(o n) -> o n", o=1).to_broadcast([P, D])).then_inc(bias_loaded, 16)
            for t in range(3, BODY):
                sp.dma_start(x_in[:, t, :], x_tiles[t]).then_inc(x_loaded[t], 16)

            def step(i, first, last):
                for j in range(BODY):
                    t = i * BODY + j
                    if not last:
                        sp.wait_ge(residual_0_ready, t + 1)
                        sp.wait_ge(residual_1_ready, t + 1)
                        sp.dma_start(x_in[:, j, :], x_tiles[t + BODY]).then_inc(x_loaded[j], 16)
                    if not (last and j == BODY - 1):
                        sp.wait_ge(out_ready, t + 1)
                        sp.dma_start(out_tiles[t], result[:, j % 2, :]).then_inc(out_stored[j % 2], 16)
                    else:
                        for h in range(2):
                            sp.wait_ge(out_ready, t + h + 1)
                            sp.dma_start(out_tiles[t][:, h * H:(h + 1) * H],
                                         result[:, j % 2, h * H:(h + 1) * H]).then_inc(out_stored[j % 2], 16)

            steps(sp, step)
            sp.wait_ge(out_stored[0], 16 * (TILES // 2))
            sp.wait_ge(out_stored[1], 16 * (TILES // 2 + 1))

        @block.gpsimd
        def _(pool):
            nc.gpsimd.memset(idle[:, :], 0.0).then_inc(idle_set, 1)
            nc.gpsimd.memset(half[:, :], 0.5).then_inc(half_set, 1)
            nc.gpsimd.memset(mixer[:, :, :], 0.0).then_inc(mixer_zeroed, 1)

            pool.wait_ge(half_set, 1)

            def step(i, first, last):
                for j in range(BODY):
                    t = i * BODY + j
                    one = slice(j % 2, j % 2 + 1)
                    if not first or j >= 2:
                        pool.wait_ge(out_stored[j % 2], 16 * (2 * i + j // 2))
                    pool.wait_ge(z_b_ready, 2 * t + 1)
                    nc.gpsimd.tensor_tensor(result[:, j % 2, 0:H], z_b[:, j % 2, 0:H], x_in[:, j, 0:H],
                                            ALU.add).then_inc(residual_0_ready, 1)
                    pool.wait_ge(m_squared, t + 1)
                    nc.gpsimd.tensor_tensor(norm_m[:, one], m_sq[:, one], half[:, :], ALU.pow).then_inc(norm_m_ready, 1)
                    pool.wait_ge(z_squared, 2 * t + 2)
                    nc.gpsimd.tensor_tensor(z_sum[:, one], z_sq[:, j % 2, 0:1], z_sq[:, j % 2, 1:2],
                                            ALU.add).then_inc(z_sum_ready, 1)
                    pool.wait_ge(z_sum_ready, t + 1)
                    nc.gpsimd.tensor_tensor(norm_z[:, one], z_sum[:, one], half[:, :], ALU.pow).then_inc(norm_z_ready, 1)

            steps(pool, step)

        @block.scalar
        def _(act):
            def split_w(k):
                act.wait_ge(w_loaded[k], 16)
                nc.scalar.copy(w_hi[:, k, :], w_in[k]).then_inc(w_hi_ready, 1)

            def split_y(j, h):
                nc.scalar.copy(y_hi[:, j // 2 % 2, h * HC:(h + 1) * HC, j % 2 * P:(j % 2 + 1) * P],
                               mix_ps[h][:, :].rearrange("p (k n) -> p k n", k=HC)).then_inc(y_hi_ready, 1)

            def make_mixer(t, j):
                for q in range(PER):
                    e = act.value_load(cond_ids[0:1, bass.ds(t * PER + q, 1)], min_val=0, max_val=E - 1)
                    part = slice(q * C, (q + 1) * C)
                    made = nc.scalar.copy(mixer[part, j % 2, q * C:(q + 1) * C],
                                          cond_all[part, bass.ds(e, 1), :].rearrange("p e d -> p (e d)"))
                made.then_inc(mixer_ready, 1)

            act.wait_ge(idle_set, 1)
            nc.scalar.activation(squares[:, 0:1], idle[:, 0:1], ACT.Square).then_inc(table_loaded, 1)
            act.wait_ge(ids_loaded, 16)
            act.wait_ge(cond_loaded, 16 * PER)
            act.wait_ge(mixer_zeroed, 1)
            for t in range(2):
                make_mixer(t, t)
            for k in range(KC):
                if k < 2:
                    act.wait_ge(mix_done, k + 1)
                    split_y(0, k)
                split_w(k)
                if k == 1:
                    make_mixer(2, 2)
                if k >= KC - 2:
                    act.wait_ge(mix_done, k - KC + 5)
                    split_y(1, k - KC + 2)
            act.wait_ge(a_loaded, 16)
            nc.scalar.copy(a_hi[:, :, :], a_in[:, :, :]).then_inc(a_hi_ready, 1)
            act.wait_ge(bm_scaled, 1)
            nc.scalar.copy(b_hi[:, :], bm_in[:, :]).then_inc(b_hi_ready, 1)

            def step(i, first, last):
                for j in range(BODY):
                    t = i * BODY + j

                    def square_z(h):
                        cols = slice(h * H, (h + 1) * H)
                        act.wait_ge(z_b_ready, 2 * t + h + 1)
                        if not first or j + h >= 1:
                            act.wait_ge(m_squared, t + h)
                        nc.scalar.activation(squares[:, cols], z_b[:, j % 2, cols], ACT.Square,
                                             accum_out=z_sq[:, j % 2, h:h + 1]).then_inc(z_squared, 1)

                    opening = first and j == 0
                    if opening:
                        act.wait_ge(mix_done, 5)
                        split_y(2, 0)
                        make_mixer(3, 3)
                    if j % 2 == 0:
                        act.wait_ge(u_done, 2 * i + j // 2 + 1)
                        nc.scalar.copy(u_hi[:, :], u_ps[:, 0:2 * P]).then_inc(u_hi_ready, 1)
                    if not opening and (not last or j + 2 < BODY):
                        act.wait_ge(mix_done, 2 * t + 5)
                        split_y(j + 2, 0)
                    if not first or j >= 2:
                        act.wait_ge(norm_z_ready, t - 1)
                    square_z(0)
                    if not opening and (not last or j + 3 < BODY):
                        act.wait_ge(mix_done, 2 * t + 4)
                        make_mixer(t + 3, j + 3)
                    act.wait_ge(m_done, t + 1)
                    if not first or j >= 2:
                        act.wait_ge(norm_m_ready, t - 1)
                    act.wait_ge(z_squared, 2 * t + 1)
                    nc.scalar.activation(squares[:, :], m_ps[:, :], ACT.Square,
                                         accum_out=m_sq[:, j % 2:j % 2 + 1]).then_inc(m_squared, 1)
                    if not last or j + 2 < BODY:
                        act.wait_ge(mix_done, 2 * t + 6)
                        split_y(j + 2, 1)
                    square_z(1)

            steps(act, step)

        @block.vector
        def _(dve):
            def split_w(k):
                dve.wait_ge(w_hi_ready, k + 1)
                nc.vector.tensor_tensor(w_lo[:, k, :], w_in[k], w_hi[:, k, :].bitcast(fp32),
                                        ALU.subtract).then_inc(w_lo_ready, 1)

            def split_y(j, h):
                part = (slice(None), j // 2 % 2, slice(h * HC, (h + 1) * HC), slice(j % 2 * P, (j % 2 + 1) * P))
                nc.vector.tensor_tensor(y_lo[part], mix_ps[h][:, :].rearrange("p (k n) -> p k n", k=HC),
                                        y_hi[part].bitcast(fp32), ALU.subtract).then_inc(y_lo_ready, 1)

            for k in range(KC):
                if k < 2:
                    dve.wait_ge(y_hi_ready, k + 1)
                    split_y(0, k)
                split_w(k)
                if k >= KC - 2:
                    dve.wait_ge(y_hi_ready, k - KC + 5)
                    split_y(1, k - KC + 2)
            dve.wait_ge(a_hi_ready, 1)
            nc.vector.tensor_tensor(a_lo[:, :, :], a_in[:, :, :], a_hi[:, :, :].bitcast(fp32),
                                    ALU.subtract).then_inc(a_lo_ready, 1)
            dve.wait_ge(bm_loaded, 16)
            dve.wait_ge(p_loaded, 16)
            nc.vector.tensor_scalar(bm_in[:, :], bm_in[:, :], p_col[:, 0:1], None, ALU.mult).then_inc(bm_scaled, 1)
            dve.wait_ge(b_hi_ready, 1)
            nc.vector.tensor_tensor(b_lo[:, :], bm_in[:, :], b_hi[:, :].bitcast(fp32),
                                    ALU.subtract).then_inc(b_lo_ready, 1)
            dve.wait_ge(bias_loaded, 16)

            def step(i, first, last):
                for j in range(BODY):
                    t = i * BODY + j
                    one = slice(j % 2, j % 2 + 1)

                    def add_bias(h):
                        cols = slice(h * H, (h + 1) * H)
                        dve.wait_ge(z_done, 2 * t + h + 1)
                        if not first or j >= 2:
                            dve.wait_ge(z_squared, 2 * t + h - 3)
                            if h == 0:
                                dve.wait_ge(residual_0_ready, t - 1)
                        nc.vector.tensor_tensor(z_b[:, j % 2, cols], z_ps[h][:, :], bias[:, cols],
                                                ALU.add).then_inc(z_b_ready, 1)

                    opening = first and j == 0
                    if opening:
                        dve.wait_ge(y_hi_ready, 5)
                        split_y(2, 0)
                    if j % 2 == 0:
                        dve.wait_ge(u_hi_ready, 2 * i + j // 2 + 1)
                        nc.vector.tensor_tensor(u_lo[:, :], u_ps[:, 0:2 * P], u_hi[:, :].bitcast(fp32),
                                                ALU.subtract).then_inc(u_lo_ready, 1)
                    if not opening and (not last or j + 2 < BODY):
                        dve.wait_ge(y_hi_ready, 2 * t + 5)
                        split_y(j + 2, 0)
                    add_bias(0)
                    if not last or j + 2 < BODY:
                        dve.wait_ge(y_hi_ready, 2 * t + 6)
                        split_y(j + 2, 1)
                    dve.wait_ge(norm_m_ready, t + 1)
                    nc.vector.tensor_scalar(twice_m[:, one], norm_m[:, one], EPS, 1.0 / CLAMP, ALU.add,
                                            ALU.mult).then_inc(twice_m_ready, 1)
                    dve.wait_ge(twice_m_ready, t + 1)
                    nc.vector.reciprocal(half_over_m[:, one], twice_m[:, one]).then_inc(over_m_ready, 1)
                    add_bias(1)
                    if not first or j >= 2:
                        dve.wait_ge(out_stored[j % 2], 16 * (2 * i + j // 2))
                    dve.wait_ge(z_b_ready, 2 * t + 2)
                    nc.vector.tensor_tensor(result[:, j % 2, H:D], z_b[:, j % 2, H:D], x_in[:, j, H:D],
                                            ALU.add).then_inc(residual_1_ready, 1)
                    dve.wait_ge(norm_z_ready, t + 1)
                    dve.wait_ge(over_m_ready, t + 1)
                    nc.vector.tensor_scalar(gamma[:, one], norm_z[:, one], half_over_m[:, one], 1.0, ALU.mult,
                                            ALU.min).then_inc(gamma_ready, 1)
                    dve.wait_ge(gamma_ready, t + 1)
                    dve.wait_ge(residual_0_ready, t + 1)
                    dve.wait_ge(residual_1_ready, t + 1)
                    parts = [slice(0, D)] if not (last and j == BODY - 1) else [slice(0, H), slice(H, D)]
                    for c in parts:
                        nc.vector.scalar_tensor_tensor(out=result[:, j % 2, c], in0=m_ps[:, c], scalar=gamma[:, one],
                                                       in1=result[:, j % 2, c], op0=ALU.mult,
                                                       op1=ALU.add).then_inc(out_ready, 1)

            steps(dve, step)

        @block.tensor
        def _(pe):
            def mix(j, h):
                for k in range(HC):
                    mixed = nc.tensor.matmul(mix_ps[h][:, k * P:(k + 1) * P],
                                             x_in[:, j % BODY, (h * HC + k) * P:(h * HC + k + 1) * P],
                                             mixer[:, j % 2, :], start=True, stop=True)
                mixed.then_inc(mix_done, 1)

            def down(j):
                g = j // 2 % 2
                for k in range(KC):
                    passes = [(a_hi, y_hi), (a_hi, y_lo), (a_lo, y_hi)]
                    for n, (left, right) in enumerate(passes):
                        summed = nc.tensor.matmul(u_ps[:, 0:2 * P], left[:, k, :], right[:, g, k, :],
                                                  start=(k == 0 and n == 0), stop=(k == KC - 1 and n == 2))
                summed.then_inc(u_done, 1)

            def linear_chunk(j, h, k):
                g, r = j // 2 % 2, slice(j % 2 * P, (j % 2 + 1) * P)
                passes = [(y_hi, w_hi), (y_hi, w_lo), (y_lo, w_hi)]
                for n, (left, right) in enumerate(passes):
                    summed = nc.tensor.matmul(z_ps[h][:, :], left[:, g, k, r], right[:, k, h * H:(h + 1) * H],
                                              start=(k == 0 and n == 0), stop=(k == KC - 1 and n == 2))
                return summed

            def linear(j, h):
                for k in range(KC):
                    summed = linear_chunk(j, h, k)
                summed.then_inc(z_done, 1)

            def up(j):
                r = slice(j % 2 * P, (j % 2 + 1) * P)
                passes = [(u_hi, b_hi), (u_hi, b_lo), (u_lo, b_hi)]
                for n, (left, right) in enumerate(passes):
                    for h in range(2):
                        c = slice(h * H, (h + 1) * H)
                        summed = nc.tensor.matmul(m_ps[:, c], left[:, r], right[:, c], start=(n == 0), stop=(n == 2))
                summed.then_inc(m_done, 1)

            pe.wait_ge(idle_set, 1)
            for _ in range(WARM):
                nc.tensor.matmul(u_ps[:, :], idle[:, 0:P], idle[:, :], start=True, stop=True)
            pe.wait_ge(x_loaded[0], 16)
            pe.wait_ge(mixer_ready, 1)
            for h in range(2):
                mix(0, h)

            for k in range(KC):
                if k % HC == 0:
                    pe.wait_ge(y_hi_ready, k // HC + 1)
                    pe.wait_ge(y_lo_ready, k // HC + 1)
                pe.wait_ge(w_hi_ready, k + 1)
                pe.wait_ge(w_lo_ready, k + 1)
                for h in range(2):
                    summed = linear_chunk(0, h, k)
                    if k == KC - 1:
                        summed.then_inc(z_done, 1)
                if k == MIX_1_AFTER:
                    pe.wait_ge(x_loaded[1], 16)
                    pe.wait_ge(mixer_ready, 2)
                    for h in range(2):
                        mix(1, h)

            pe.wait_ge(x_loaded[2], 16)
            pe.wait_ge(mixer_ready, 3)
            pe.wait_ge(y_lo_ready, 3)
            mix(2, 0)
            pe.wait_ge(y_hi_ready, 4)
            pe.wait_ge(y_lo_ready, 4)
            pe.wait_ge(a_hi_ready, 1)
            pe.wait_ge(a_lo_ready, 1)
            down(0)
            mix(2, 1)
            pe.wait_ge(b_hi_ready, 1)
            pe.wait_ge(b_lo_ready, 1)
            pe.wait_ge(u_hi_ready, 1)
            pe.wait_ge(u_lo_ready, 1)
            up(0)

            def step(i, first, last):
                for j in range(BODY):
                    t = i * BODY + j
                    if first and j == 0:
                        continue

                    if j % 2 == 0:
                        pe.wait_ge(y_hi_ready, 2 * t + 4)
                        pe.wait_ge(y_lo_ready, 2 * t + 4)
                        pe.wait_ge(u_lo_ready, 2 * i + j // 2)
                        down(j)
                    if not last or j + 2 < BODY:
                        pe.wait_ge(x_loaded[(j + 2) % BODY], 16 * (i + (j + 2) // BODY + 1))
                        pe.wait_ge(mixer_ready, t + 3)
                        pe.wait_ge(y_lo_ready, 2 * t + 3)
                        mix(j + 2, 0)
                    pe.wait_ge(z_b_ready, 2 * t - 1)
                    linear(j, 0)
                    pe.wait_ge(u_hi_ready, 2 * i + j // 2 + 1)
                    pe.wait_ge(u_lo_ready, 2 * i + j // 2 + 1)
                    pe.wait_ge(out_ready, t)
                    up(j)
                    if not last or j + 2 < BODY:
                        pe.wait_ge(y_lo_ready, 2 * t + 4)
                        mix(j + 2, 1)
                    pe.wait_ge(z_b_ready, 2 * t)
                    linear(j, 1)

            steps(pe, step)


_INS = ['x', 'itok_B_0_15', 'L0_cond_weights', 'L0_ffn_W', 'L0_ffn_b', 'L0_ffn_A', 'L0_ffn_B', 'L0_ffn_p_scores']


def kernel(**inputs):
    import numpy as _np
    import concourse.bacc as _bacc
    from concourse import mybir as _mybir
    from concourse.bass_utils import run_bass_kernel_spmd as _run

    nc = _bacc.Bacc("TRN2", target_bir_lowering=False, num_devices=1)
    arrays, args = {}, []
    laid_out = dict(inputs)
    laid_out['L0_ffn_W'] = _np.transpose(inputs['L0_ffn_W'])
    laid_out['L0_ffn_A'] = _np.transpose(inputs['L0_ffn_A'], (1, 0, 2))
    laid_out['L0_cond_weights'] = _np.transpose(inputs['L0_cond_weights'], (1, 0, 2))
    for name in _INS:
        a = _np.ascontiguousarray(laid_out[name])
        arrays[f"in_{name}_dram"] = a
        args.append(nc.dram_tensor(f"in_{name}_dram", a.shape, _mybir.dt.from_np(a.dtype), kind="ExternalInput").ap())
    shape = inputs['x'].shape
    args.append(nc.dram_tensor("out_0_dram", shape, _mybir.dt.float32, kind="ExternalOutput").ap())
    conditioned_clamped_low_rank_linear_kernel(nc, *args)
    r = _run(nc, [arrays], core_ids=[0])
    return r.results[0]["out_0_dram"]
```
